# Optimizing a Trainium2 kernel written in Bass

```python
import numpy as np
import jax
import jax.numpy as jnp

def _softmax(x, axis=-1):
    return jax.nn.softmax(x, axis=axis)

def _gelu(x):
    return jax.nn.gelu(x, approximate=True)

def _silu(x):
    return jax.nn.silu(x)

def _sigmoid(x):
    return jax.nn.sigmoid(x)

def _layernorm(x, axis=-1, eps=1e-05):
    m = jnp.mean(x, axis=axis, keepdims=True)
    v = jnp.var(x, axis=axis, keepdims=True)
    return (x - m) / jnp.sqrt(v + eps)

def _scatter_add(tgt, idx, src, axis=0):
    return tgt.at[idx].add(src)

def _segment_sum(src, seg, n):
    return jax.ops.segment_sum(src, seg, n)
kernel_name = 'mk_gps_d1_gnn_r8_630044'

def setup_inputs(seed: int=0):
    np.random.seed(seed)
    _w = jnp.asarray

    def _rec_inputs():
        import jax
        import jax.numpy as jnp
        _gk = jax.random.key(seed)
        x = -0.003407 + 1.001 * jax.random.normal(jax.random.fold_in(_gk, 1), (6250, 256), jnp.float32)
        _s = jax.random.randint(jax.random.fold_in(_gk, 2), (100000,), 0, 6250, jnp.int32)
        _d = jax.random.randint(jax.random.fold_in(_gk, 3), (100000,), 0, 6250, jnp.int32)
        _loop = jnp.arange(6250, dtype=jnp.int32)
        src = jnp.concatenate([_s, _d, _loop])
        dst = jnp.concatenate([_d, _s, _loop])
        _o = jnp.argsort(dst, stable=True)
        src = src[_o]
        dst = dst[_o]
        edge_weight1 = jax.random.uniform(jax.random.fold_in(_gk, 12), (206250, 1), jnp.float32, 0.0, 1)
        return (x, src, dst, edge_weight1)
    x, src, dst, edge_weight1 = _rec_inputs()

    def _L0_gnn_setup():
        import jax, jax.numpy as jnp
        import numpy as np
        BS = 512
        EMBED = 256
        NHEAD = 8
        HDIM = EMBED // NHEAD
        E = BS * BS

        def _xavier(key, shape):
            lim = float(np.sqrt(6.0 / (shape[0] + shape[1])))
            return jax.random.uniform(key, shape, jnp.float32, -lim, lim)
        key = jax.random.key(seed)
        ks = jax.random.split(key, 6)
        feats = jax.random.normal(ks[0], (BS, EMBED), jnp.float32)
        dst = jnp.repeat(jnp.arange(BS), BS)
        src = jnp.tile(jnp.arange(BS), BS)
        edge_index = jnp.stack([src, dst], axis=1).astype(jnp.int32)
        edge_attr = jnp.zeros((E, 1), jnp.float32)
        return {'feats': feats, 'edge_index': edge_index, 'edge_attr': edge_attr, 'Wq': _xavier(ks[1], (EMBED, EMBED)), 'bq': jnp.zeros((EMBED,), jnp.float32), 'Wk': _xavier(ks[2], (EMBED, EMBED)), 'bk': jnp.zeros((EMBED,), jnp.float32), 'Wv': _xavier(ks[3], (EMBED, EMBED)), 'bv': jnp.zeros((EMBED,), jnp.float32), 'Wo': _xavier(ks[4], (EMBED, EMBED)), 'bo': jnp.zeros((EMBED,), jnp.float32)}
    _L0_gnn_all = _L0_gnn_setup()
    _L0_gnn_in = {k: v for k, v in _L0_gnn_all.items() if k in ('Wq', 'bq', 'Wk', 'bk', 'Wv', 'bv', 'Wo', 'bo')}
    del _L0_gnn_all

    def _L0_mix_setup():
        import jax, jax.numpy as jnp
        import numpy as np
        HEADS, DIM_HEAD = (8, 64)
        EPS = 1e-05

        def instance_norm(t):
            mu = jnp.mean(t, axis=-1, keepdims=True)
            var = jnp.mean((t - mu) ** 2, axis=-1, keepdims=True)
            return (t - mu) * jax.lax.rsqrt(var + EPS)
        key = jax.random.key(seed)
        k1, k2, k3, k4 = jax.random.split(key, 4)
        B, N, D = (8, 1024, 256)
        inner = HEADS * DIM_HEAD
        x = jax.random.normal(k1, (B, N, D), jnp.float32)
        w_qkv = jax.random.normal(k2, (3 * inner, D), jnp.float32) / np.sqrt(D).astype(np.float32)
        w_out = jax.random.normal(k3, (D, inner), jnp.float32) / np.sqrt(inner).astype(np.float32)
        b_out = 0.01 * jax.random.normal(k4, (D,), jnp.float32)
        return {'x': x, 'w_qkv': w_qkv, 'w_out': w_out, 'b_out': b_out}
    _L0_mix_all = _L0_mix_setup()
    _L0_mix_in = {k: v for k, v in _L0_mix_all.items() if k in ('w_qkv', 'w_out', 'b_out')}
    del _L0_mix_all

    def _L0_ffn_setup():
        import math
        import jax, jax.numpy as jnp
        import numpy as np
        CAPACITY_FACTOR = 1.25
        key = jax.random.key(seed)
        ks = jax.random.split(key, 5)
        B, L, D, F, E = (8, 1024, 256, 1024, 8)
        h = jax.random.normal(ks[0], (B, L, D), dtype=jnp.float32)
        gate_w = jax.random.normal(ks[1], (D, E), dtype=jnp.float32) * 0.02
        gate_b = jnp.zeros((E,), dtype=jnp.float32)
        w1 = jax.random.normal(ks[2], (E, D, F), dtype=jnp.float32) * (1.0 / math.sqrt(D))
        b1 = jnp.zeros((E, F), dtype=jnp.float32)
        w2 = jax.random.normal(ks[3], (E, F, D), dtype=jnp.float32) * (1.0 / math.sqrt(F))
        b2 = jnp.zeros((E, D), dtype=jnp.float32)
        return {'h': h, 'gate_w': gate_w, 'gate_b': gate_b, 'w1': w1, 'b1': b1, 'w2': w2, 'b2': b2}
    _L0_ffn_all = _L0_ffn_setup()
    _L0_ffn_in = {k: v for k, v in _L0_ffn_all.items() if k in ('gate_w', 'gate_b', 'w1', 'b1', 'w2', 'b2')}
    del _L0_ffn_all
    return {'x': x, 'src': src, 'dst': dst, 'edge_weight1': edge_weight1, 'L0_gnn_Wq': _L0_gnn_in['Wq'], 'L0_gnn_bq': _L0_gnn_in['bq'], 'L0_gnn_Wk': _L0_gnn_in['Wk'], 'L0_gnn_bk': _L0_gnn_in['bk'], 'L0_gnn_Wv': _L0_gnn_in['Wv'], 'L0_gnn_bv': _L0_gnn_in['bv'], 'L0_gnn_Wo': _L0_gnn_in['Wo'], 'L0_gnn_bo': _L0_gnn_in['bo'], 'L0_mix_w_qkv': _L0_mix_in['w_qkv'], 'L0_mix_w_out': _L0_mix_in['w_out'], 'L0_mix_b_out': _L0_mix_in['b_out'], 'L0_ffn_gate_w': _L0_ffn_in['gate_w'], 'L0_ffn_gate_b': _L0_ffn_in['gate_b'], 'L0_ffn_w1': _L0_ffn_in['w1'], 'L0_ffn_b1': _L0_ffn_in['b1'], 'L0_ffn_w2': _L0_ffn_in['w2'], 'L0_ffn_b2': _L0_ffn_in['b2']}

def reference(x, src, dst, edge_weight1, L0_gnn_Wq, L0_gnn_bq, L0_gnn_Wk, L0_gnn_bk, L0_gnn_Wv, L0_gnn_bv, L0_gnn_Wo, L0_gnn_bo, L0_mix_w_qkv, L0_mix_w_out, L0_mix_b_out, L0_ffn_gate_w, L0_ffn_gate_b, L0_ffn_w1, L0_ffn_b1, L0_ffn_w2, L0_ffn_b2):
    import jax
    import jax.numpy as jnp

    def _L0_gnn_ref(feats, edge_index, edge_attr, Wq, bq, Wk, bk, Wv, bv, Wo, bo):
        import jax, jax.numpy as jnp
        import numpy as np
        BS = 512
        EMBED = 256
        NHEAD = 8
        HDIM = EMBED // NHEAD
        E = BS * BS

        def _xavier(key, shape):
            lim = float(np.sqrt(6.0 / (shape[0] + shape[1])))
            return jax.random.uniform(key, shape, jnp.float32, -lim, lim)
        bs = feats.shape[0]
        scale = 1.0 / np.sqrt(HDIM)
        q = (feats @ Wq.T + bq).reshape(bs, NHEAD, HDIM).transpose(1, 0, 2)
        k = (feats @ Wk.T + bk).reshape(bs, NHEAD, HDIM).transpose(1, 0, 2)
        v = (feats @ Wv.T + bv).reshape(bs, NHEAD, HDIM).transpose(1, 0, 2)
        r, c = (edge_index[:, 0], edge_index[:, 1])
        qe = q[:, c, :]
        ke = k[:, r, :]
        ve = v[:, r, :]
        sim = jnp.einsum('hed,hed->eh', qe, ke) * scale
        m = jax.ops.segment_max(sim, c, num_segments=bs)
        p = jnp.exp(sim - m[c])
        s = jax.ops.segment_sum(p, c, num_segments=bs)
        attn = p / s[c]
        out_e = attn.T[..., None] * ve
        out_e = out_e.transpose(1, 0, 2).reshape(-1, NHEAD * HDIM)
        agg = jax.ops.segment_sum(out_e, c, num_segments=bs)
        return agg @ Wo.T + bo

    def _L0_mix_ref(x, w_qkv, w_out, b_out):
        import jax, jax.numpy as jnp
        import numpy as np
        HEADS, DIM_HEAD = (8, 64)
        EPS = 1e-05

        def instance_norm(t):
            mu = jnp.mean(t, axis=-1, keepdims=True)
            var = jnp.mean((t - mu) ** 2, axis=-1, keepdims=True)
            return (t - mu) * jax.lax.rsqrt(var + EPS)
        B, N, _ = x.shape
        H, Dh = (HEADS, DIM_HEAD)
        qkv = jnp.einsum('bnd,ed->bne', x, w_qkv)
        q, k, v = jnp.split(qkv, 3, axis=-1)

        def to_heads(t):
            return t.reshape(B, N, H, Dh).transpose(0, 2, 1, 3)
        q, k, v = (to_heads(q), to_heads(k), to_heads(v))
        k = instance_norm(k)
        v = instance_norm(v)
        dots = jnp.einsum('bhnd,bhne->bhde', k, v)
        out = jnp.einsum('bhnd,bhde->bhne', q, dots) / N
        out = out.transpose(0, 2, 1, 3).reshape(B, N, H * Dh)
        return jnp.einsum('bne,de->bnd', out, w_out) + b_out

    def _L0_ffn_ref(h, gate_w, gate_b, w1, b1, w2, b2):
        import math
        import jax, jax.numpy as jnp
        import numpy as np
        CAPACITY_FACTOR = 1.25
        B, L, D = h.shape
        E = gate_w.shape[1]
        T = B * L
        C = max(1, math.ceil(CAPACITY_FACTOR * T / E))
        x = h.reshape(T, D)
        logits = x @ gate_w + gate_b
        probs = jax.nn.softmax(logits, axis=-1)
        idx = jnp.argmax(probs, axis=-1)
        prb = jnp.take_along_axis(probs, idx[:, None], axis=1)[:, 0]
        one_hot = jax.nn.one_hot(idx, E, dtype=jnp.float32)
        pos = (jnp.cumsum(one_hot, axis=0) * one_hot).sum(-1).astype(jnp.int32) - 1
        kept = pos < C
        pos_safe = jnp.where(kept, pos, C)
        buf = jnp.zeros((E, C, D), dtype=h.dtype).at[idx, pos_safe].set(x, mode='drop')
        hmid = jax.nn.relu(jnp.einsum('ecd,edf->ecf', buf, w1) + b1[:, None, :])
        ybuf = jnp.einsum('ecf,efd->ecd', hmid, w2) + b2[:, None, :]
        pos_g = jnp.minimum(pos, C - 1)
        y_tok = ybuf[idx, pos_g] * (prb * kept)[:, None]
        y = y_tok.reshape(B, L, D)
        y = jnp.nan_to_num(y, nan=0.0, posinf=10000.0, neginf=-10000.0)
        return y
    edge_index_t = jnp.stack([src, dst], axis=1)
    xn = _layernorm(x, axis=-1)
    x = x + _L0_gnn_ref(xn, edge_index_t, edge_weight1, L0_gnn_Wq, L0_gnn_bq, L0_gnn_Wk, L0_gnn_bk, L0_gnn_Wv, L0_gnn_bv, L0_gnn_Wo, L0_gnn_bo) + _L0_mix_ref(xn[None], L0_mix_w_qkv, L0_mix_w_out, L0_mix_b_out)[0]
    x = x + _L0_ffn_ref(_layernorm(x, axis=-1)[None], L0_ffn_gate_w, L0_ffn_gate_b, L0_ffn_w1, L0_ffn_b1, L0_ffn_w2, L0_ffn_b2)[0]
    return x

_drawn_inputs = setup_inputs


def setup_inputs(seed=0):
    import zlib

    import numpy as np

    out = dict(_drawn_inputs(seed))
    spreads = {'L0_gnn_bq': (0.0, 0.271),
     'L0_gnn_bk': (0.0, 0.8),
     'L0_gnn_bv': (0.0, 0.1),
     'L0_gnn_bo': (0.0, 0.1),
     'L0_ffn_gate_b': (0.0, 0.1),
     'L0_ffn_b1': (0.0, 0.7),
     'L0_ffn_b2': (0.0, 0.498)}
    factors = {'L0_mix_b_out': 4.685}
    for name, (base, spread) in spreads.items():
        noise = np.random.default_rng([zlib.crc32(name.encode()), seed]).standard_normal(out[name].shape)
        drawn = base * np.exp(spread * noise) if base else spread * noise
        out[name] = jnp.asarray(drawn.astype(out[name].dtype))
    for name, factor in factors.items():
        out[name] = (out[name] * factor).astype(out[name].dtype)
    return out
```

```python
import concourse.bass as bass
from concourse import mybir
from contextlib import ExitStack

N = 6250
NT = 49
NP = NT * 128
E = 206250
NB = 1612
NBP = 1664
EP = NBP * 128
D = 256
H = 8
C = 977
CP = 1024
J = 8
BLK = 64
EPS = 1e-5
BIG = 1e30


class Sem:

    def __init__(self, handle):
        self.h = handle
        self.n = 0

    def inc(self, ins, k=1):
        ins.then_inc(self.h, k)
        self.n += k
        return (self, self.n)


class Waits:

    def __init__(self):
        self.seen = {}

    def __call__(self, eng, *tokens):
        for tok in tokens:
            if tok is None:
                continue
            s, v = tok
            key = (id(eng), id(s))
            if self.seen.get(key, 0) < v:
                eng.wait_ge(s.h, v)
                self.seen[key] = v


def gps_layer_kernel(nc, x, src, dst, wall, ball, wmix, wqm, wout, wo, bo, b_out, gate_w, gate_b, w1, b1, w2, b2, out):
    f32 = mybir.dt.float32
    bf16 = mybir.dt.bfloat16
    i32 = mybir.dt.int32
    ALU = mybir.AluOpType
    ACT = mybir.ActivationFunctionType
    AX = mybir.AxisListType
    V, S, T, G, Y = nc.vector, nc.scalar, nc.tensor, nc.gpsimd, nc.sync

    ctx = ExitStack()
    with ctx:
        sems = {}

        def sem(name):
            sems[name] = Sem(ctx.enter_context(nc.semaphore(name)))
            return sems[name]

        A = ctx.enter_context(nc.sbuf_tensor("arena", [128, 52800], f32))
        top = [0]

        def take(n):
            top[0] += n
            assert top[0] <= 52800, top[0]
            return A[:, top[0] - n:top[0]]

        def r3(ap, b):
            return ap.rearrange("p (a b) -> p a b", b=b)

        def dram(name, shape, dt=f32):
            return nc.dram_tensor(name, shape, dt, kind="Internal").ap()

        ps = [ctx.enter_context(nc.psum_tensor(f"ps{i}", [128, 512], f32)) for i in range(8)]
        kv_d = dram("kv_d", [NP, 512])
        q_d = dram("q_d", [NP, D])
        dst_d = dram("dst_d", [NBP, 128], i32)
        src_d = dram("src_d", [NBP, 128], i32)
        tab_d = dram("tab_d", [NP, 4], i32)
        agg_d = dram("agg_d", [NP, D])
        hb_d = dram("hb_d", [H * CP, D])
        yb_d = dram("yb_d", [H * C, D])

        sv, sa, sp, sg = sem("sv"), sem("sa"), sem("sp"), sem("sg")
        wait = Waits()

        def v(ins):
            return sv.inc(ins)

        def a(ins):
            return sa.inc(ins)

        def g(ins):
            return sg.inc(ins)

        def dma(eng, o, i, s, **kw):
            return s.inc(eng.dma_start(o, i, **kw), 16)

        R0 = take(12544)
        R1 = take(12800)
        R2 = take(16384)
        R3 = take(4480)
        IDX = take(3200)
        xnT = R0.rearrange("p (k n) -> p k n", k=2)

        ident, tri, ones = take(128), take(128), take(128)
        iota = take(128)
        wo_s = r3(take(512), 256)
        M = r3(take(512), 256)
        gbias = take(8)
        gw = r3(take(16), 8)
        e0 = take(1)
        nodeid = take(50)
        degS, rpS = take(50), take(50)
        nch = take(64).bitcast(i32)
        permS = take(50).bitcast(i32)
        slotS = take(50).bitcast(i32)
        slotG = take(50).bitcast(i32)
        coef = take(50)
        valid = take(1)
        qring = [take(256) for _ in range(2)]
        ixring = [take(BLK).bitcast(i32) for _ in range(2)]
        degring = [take(1) for _ in range(2)]
        rpring = [take(1) for _ in range(2)]
        maskb = take(BLK)
        offi = take(1).bitcast(i32)
        offf = take(1)
        acc = take(264)
        Sb = take(72)
        Db = take(72)
        mnew = take(8)
        rin = take(8)

        pre = [512]

        def temp(n):
            pre[0] += n
            assert pre[0] <= 2048
            return R3[:, pre[0] - n:pre[0]]

        trib = temp(64).bitcast(bf16)
        onesb = temp(64).bitcast(bf16)
        tabS = temp(NT * 4).bitcast(i32).rearrange("p (t c) -> p t c", c=4)
        rank = temp(50).bitcast(i32)
        sml = [temp(64) for _ in range(3)]

        t_c = g(G.memset(ident, 0.0))
        t_c1 = g(G.memset(tri, 1.0))
        t_c2 = g(G.memset(ones, 1.0))
        wait(G, t_c2)
        t_id = g(G.affine_select(out=ident, in_=ident, compare_op=ALU.not_equal, fill=1.0, base=0,
                                 pattern=[[-1, 128]], channel_multiplier=1))
        t_tri = g(G.affine_select(out=tri, in_=tri, compare_op=ALU.is_gt, fill=0.0, base=0,
                                  pattern=[[1, 128]], channel_multiplier=-1))
        io_i = sml[0].bitcast(i32)
        t_io = g(G.iota(R3[:, 0:128].bitcast(i32), pattern=[[1, 128]], base=0, channel_multiplier=0))
        t_nd = g(G.iota(io_i[:, 0:50], pattern=[[1, 50]], base=0, channel_multiplier=NT))
        t_pp = g(G.iota(io_i[:, 50:51], pattern=[[0, 1]], base=0, channel_multiplier=1))
        wait(V, t_pp, t_tri, t_id)
        v(V.tensor_copy(iota, R3[:, 0:128].bitcast(i32)))
        v(V.tensor_copy(nodeid, io_i[:, 0:50]))
        v(V.tensor_copy(trib, tri))
        v(V.tensor_copy(onesb, ones))
        t_k = v(V.tensor_copy(e0, io_i[:, 50:51]))
        wait(V, t_k)
        v(V.tensor_scalar(out=valid, in0=e0, scalar1=float(N - 48 * 128), scalar2=None, op0=ALU.is_lt))
        t_const = v(V.tensor_scalar(out=e0, in0=e0, scalar1=0.0, scalar2=None, op0=ALU.is_equal))

        s_pad, s_ed, s_fi = sem("s_pad"), sem("s_ed"), sem("s_fi")
        zero = R3[:, 2048:2048 + 2048]
        bigi = R3[:, 128:256].bitcast(i32)
        t_z = v(V.memset(zero, 0.0))
        t_b = v(V.memset(bigi, 1 << 20))
        flat = lambda d: d.rearrange("a b -> (a b)")
        npad = EP - E
        dma(Y, flat(dst_d)[0:E].rearrange("(a b) -> a b", b=825), dst.rearrange("(a b) -> a b", b=825), s_ed)
        wait(Y, t_b)
        dma(Y, flat(dst_d)[E:E + 86].rearrange("(a b) -> a b", a=1), bigi[0:1, 0:86], s_ed)
        t_ed = dma(Y, dst_d[NB:NBP, :], bigi[0:NBP - NB, :], s_ed)
        assert E + 86 == NB * 128
        firsts = temp(13)
        fi_i = temp(13).bitcast(i32)
        wait(Y, t_ed)
        t_fi = dma(Y, fi_i, dst_d.rearrange("(a p) j -> p a j", p=128)[:, :, 0], s_fi, allow_slow_non_contiguous=True)

        xbuf = [r3(R2[:, 6400 + i * 1792:6400 + (i + 1) * 1792], 256) for i in range(2)]
        s_x = [sem("s_x0"), sem("s_x1")]

        def load_x(grp):
            b = grp % 2
            if grp < 6:
                r = x[grp * 896:(grp + 1) * 896, :].rearrange("(t p) d -> p t d", p=128)
                return dma(Y, xbuf[b], r, s_x[b])
            r = x[grp * 896:grp * 896 + 768, :].rearrange("(t p) d -> p t d", p=128)
            dma(Y, xbuf[b][:, 0:6, :], r, s_x[b])
            return dma(Y, xbuf[b][0:N - 48 * 128, 6, :], x[48 * 128:N, :], s_x[b])

        t_x = {0: load_x(0)}
        s_w = sem("s_w")
        W = r3(R2[:, 0:1536], 768)
        bal = R2[:, 1536:2304]
        wmx = r3(R2[:, 2304:4352], 1024)
        wq_s = r3(R2[:, 4352:5376], 256)
        wou_s = r3(R2[:, 5376:6400], 256)
        kpart = lambda w: w.rearrange("(k p) n -> p k n", p=128)
        row = lambda b: b.rearrange("(a n) -> a n", a=1)
        dma(Y, W, kpart(wall), s_w)
        t_w = dma(Y, bal, row(ball).to_broadcast([128, 768]), s_w)
        t_x[1] = load_x(1)
        s_w2 = sem("s_w2")
        dma(Y, wmx, kpart(wmix), s_w2)
        dma(Y, wq_s, kpart(wqm), s_w2)
        dma(Y, wou_s, kpart(wout), s_w2)
        dma(Y, wo_s, kpart(wo), s_w2)
        dma(Y, gw, kpart(gate_w), s_w2)
        dma(Y, gbias, row(gate_b).to_broadcast([128, 8]), s_w2)
        t_w2 = (s_w2, s_w2.n)
        s_pz = sem("s_pz")
        dma(Y, flat(src_d)[0:E].rearrange("(a b) -> a b", b=825), src.rearrange("(a b) -> a b", b=825), s_pz)
        wait(Y, t_z)
        dma(Y, flat(src_d)[E:E + 86].rearrange("(a b) -> a b", a=1), zero[0:1, 0:86].bitcast(i32), s_pz)
        t_src = dma(Y, src_d[NB:NBP, :], zero[0:NBP - NB, 0:128].bitcast(i32), s_pz)
        s_hz = sem("s_hz")
        for i in range(8):
            t_hz = dma(Y, hb_d[i * CP:(i + 1) * CP, :].rearrange("(p j) d -> p (j d)", p=128), zero, s_hz)

        Fr = R1[:, 0:NBP]
        diag = R1[:, NBP:2 * NBP]
        junk = R1[:, NBP:2 * NBP]
        wait(V, t_fi, t_const)
        t = v(V.tensor_copy(firsts, fi_i))
        wait(V, t, t_id)
        t_dg = v(V.tensor_tensor(r3(diag, 128), ident.unsqueeze(1).to_broadcast([128, 13, 128]),
                                 firsts.unsqueeze(2).to_broadcast([128, 13, 128]), ALU.mult))
        wait(T, t_dg, t_c2)
        for i in range(4):
            w_ = min(512, NBP - 512 * i)
            t_f = sp.inc(T.matmul(ps[i][:, 0:w_], ones, diag[:, 512 * i:512 * i + w_], start=True, stop=True))
        wait(V, t_f)
        for i in range(4):
            w_ = min(512, NBP - 512 * i)
            t_F = v(V.tensor_copy(Fr[:, 512 * i:512 * i + w_], ps[i][:, 0:w_]))
        cnt = temp(50)

        last_junk = [t_F]

        def compare(c):
            wait(V, last_junk[0])
            last_junk[0] = v(V.tensor_scalar(out=junk, in0=Fr, scalar1=nodeid[:, c:c + 1], scalar2=0.0,
                                             op0=ALU.is_lt, op1=ALU.add, accum_out=cnt[:, c:c + 1]))

        st = take(42)
        mv = take(14)
        rs = take(7)
        wait(V, t_w)
        v(V.tensor_scalar(out=W[:, :, 512:768], in0=W[:, :, 512:768], scalar1=32.0 ** -0.5, scalar2=None, op0=ALU.mult))
        t_W = v(V.tensor_scalar(out=bal[:, 512:768], in0=bal[:, 512:768], scalar1=32.0 ** -0.5, scalar2=None, op0=ALU.mult))

        def norm(xt, n, o=None):
            o = xt if o is None else o
            last = None
            for j in range(n):
                last = v(V.bn_stats(st[:, 6 * j:6 * j + 6], xt[:, j, :]))
            wait(V, last)
            for j in range(n):
                last = v(V.bn_aggr(mv[:, 2 * j:2 * j + 2], st[:, 6 * j:6 * j + 6]))
            wait(V, last)
            last = v(V.tensor_scalar(out=rs[:, 0:n], in0=r3(mv, 2)[:, 0:n, 1], scalar1=EPS, scalar2=None, op0=ALU.add))
            wait(S, last)
            last = a(S.activation(rs[:, 0:n], rs[:, 0:n], ACT.Sqrt))
            wait(V, last)
            last = v(V.reciprocal(rs[:, 0:n], rs[:, 0:n]))
            wait(V, last)
            for j in range(n):
                last = v(V.tensor_scalar(out=o[:, j, :], in0=xt[:, j, :], scalar1=mv[:, 2 * j:2 * j + 1],
                                         scalar2=rs[:, j:j + 1], op0=ALU.subtract, op1=ALU.mult))
            return last

        stage = [R2[:, 9984 + 768 * i:9984 + 768 * (i + 1)] for i in range(3)]
        s_st = [sem(f"s_st{i}") for i in range(3)]
        t_st = [None] * 3
        t_ev = {}
        t_xT = {}
        t_tp = {}
        t_bias = {}
        t_n = {}
        wait(V, t_x[0])
        t_n[0] = norm(xbuf[0], 7)
        ncmp = 0
        for grp in range(7):
            if grp + 1 < 7:
                wait(V, t_x[grp + 1])
                t_n[grp + 1] = norm(xbuf[(grp + 1) % 2], 7)
            for j in range(7):
                t = grp * 7 + j
                pt = ps[6 + t % 2]
                wait(T, t_n[grp], t_xT.get(t - 2), t_id)
                for k in range(2):
                    t_tp[t] = sp.inc(T.transpose(pt[:, k * 128:(k + 1) * 128], xbuf[grp % 2][:, j, k * 128:(k + 1) * 128], ident))
                wait(S, t_tp[t])
                t_xT[t] = a(S.activation(xnT[:, :, t * 128:(t + 1) * 128], r3(pt[:, 0:256], 128), ACT.Copy))
                if t > 0:
                    tiles = [t - 1]
                else:
                    tiles = []
                if t == NT - 1:
                    tiles.append(t)
                for u in tiles:
                    b0, b1_ = ps[2 * (u % 2)], ps[2 * (u % 2) + 1]
                    wait(T, t_xT[u], t_bias.get(u - 2), t_W, t_F)
                    for k in range(2):
                        T.matmul(b0[:, :], xnT[:, k, u * 128:(u + 1) * 128], W[:, k, 0:512], start=(k == 0), stop=(k == 1))
                    for k in range(2):
                        m = T.matmul(b1_[:, 0:256], xnT[:, k, u * 128:(u + 1) * 128], W[:, k, 512:768], start=(k == 0), stop=(k == 1))
                    tm = sp.inc(m)
                    wait(V, tm, t_st[u % 3])
                    v(V.tensor_tensor(stage[u % 3][:, 0:512], b0[:, :], bal[:, 0:512], ALU.add))
                    t_bias[u] = v(V.tensor_tensor(stage[u % 3][:, 512:768], b1_[:, 0:256], bal[:, 512:768], ALU.add))
                    wait(Y, t_bias[u])
                    dma(Y, kv_d[u * 128:(u + 1) * 128, :], stage[u % 3][:, 0:512], s_st[u % 3])
                    t_st[u % 3] = dma(Y, q_d[u * 128:(u + 1) * 128, :], stage[u % 3][:, 512:768], s_st[u % 3])
                    compare(ncmp)
                    ncmp += 1
            if grp + 2 < 7:
                if grp + 2 == 6:
                    wait(V, t_tp[grp * 7 + 6])
                    wait(Y, v(V.memset(xbuf[0][:, 6, :], 0.0)))
                wait(Y, t_tp[grp * 7 + 6])
                t_x[grp + 2] = load_x(grp + 2)
        compare(ncmp)
        t_kv = list(t_st)

        blk = temp(50)
        blki = temp(50).bitcast(i32)
        wait(V, last_junk[0])
        t = v(V.tensor_scalar(out=blk, in0=cnt, scalar1=-1.0, scalar2=0.0, op0=ALU.add, op1=ALU.max))
        wait(V, t)
        t_blk = v(V.tensor_copy(blki, blk))
        rows = R1[:, 2 * NBP:2 * NBP + 6400].bitcast(i32).rearrange("p (t j) -> p t j", j=128)
        s_row = sem("s_row")
        wait(G, t_blk, t_ed)
        for c in range(50):
            t_row = s_row.inc(G.indirect_dma_start(out=rows[:, c, :], out_offset=None, in_=dst_d,
                                                   in_offset=bass.IndirectOffsetOnAxis(ap=blki[:, c:c + 1], axis=0)), 16)
        less = r3(R1[:, 0:3200].bitcast(bf16), 128)
        fine, rp, deg = temp(50), temp(50), temp(50)

        def rank_1():
            wait(V, t_row, last_junk[0])
            t = v(V.tensor_tensor(less, rows, nodeid.unsqueeze(2).to_broadcast([128, 50, 128]), ALU.is_lt))
            wait(V, t)
            t = v(V.tensor_reduce(fine, less, AX.X, ALU.add))
            wait(V, t)
            t = v(V.scalar_tensor_tensor(out=rp, in0=blk, scalar=128.0, in1=fine, op0=ALU.mult, op1=ALU.add))
            wait(V, t)
            t = v(V.tensor_tensor(deg[:, 0:NT], rp[:, 1:50], rp[:, 0:NT], ALU.subtract))
            wait(V, t)
            t = v(V.tensor_scalar(out=fine[:, 0:NT], in0=deg[:, 0:NT], scalar1=-1.0, scalar2=127.0, op0=ALU.mult, op1=ALU.add))
            wait(V, t)
            t = v(V.tensor_scalar(out=fine[:, 0:NT], in0=fine[:, 0:NT], scalar1=0.0, scalar2=None, op0=ALU.max))
            wait(V, t)
            return v(V.tensor_tensor(OH, iota.unsqueeze(1).to_broadcast([128, NT, 128]),
                                     fine[:, 0:NT].unsqueeze(2).to_broadcast([128, NT, 128]), ALU.is_equal))

        OH = r3(R1[:, 0:3136].bitcast(bf16), 128)
        RR = r3(R1[:, 3200:3200 + NT * 128], 128)
        prod_r = R1[:, 9600:10112]
        tot = R1[:, 10112:10240]
        inc_ = R1[:, 10240:10368]
        base = R1[:, 10368:10496]
        rankf = temp(50)

        def rank_2(t_oh, bank):
            wait(T, t_oh)
            for c in range(NT):
                m = T.matmul(bank[:, 0:128], onesb, OH[:, c, :], start=(c == 0), stop=(c == NT - 1))
            t = sp.inc(m)
            wait(V, t)
            t = v(V.tensor_copy(tot, bank[:, 0:128]))
            wait(V, t)
            t = v(V.tensor_tensor_scan(inc_, tot, tot, 0.0, ALU.add, ALU.bypass))
            wait(V, t)
            t = v(V.tensor_tensor(base, inc_, tot, ALU.subtract))
            wait(V, t)
            t = v(V.tensor_scalar(out=RR[:, 0, :], in0=base, scalar1=e0, scalar2=None, op0=ALU.mult))
            for c in range(NT - 1):
                wait(V, t)
                t = v(V.tensor_tensor(RR[:, c + 1, :], RR[:, c, :], OH[:, c, :], ALU.add))
            return t

        def rank_3(t_rr, banks):
            wait(T, t_rr)
            tr = [None, None]
            for q in range(13):
                n = min(4, NT - 4 * q)
                b = banks[q % 2]
                wait(T, tr[q % 2])
                for i in range(n):
                    c = 4 * q + i
                    T.matmul(b[:, i * 128:(i + 1) * 128], ones, RR[:, c, :], start=True, stop=False)
                    m = T.matmul(b[:, i * 128:(i + 1) * 128], trib, OH[:, c, :], start=False, stop=True)
                t = sp.inc(m)
                wait(V, t, last_rank[0])
                tr[q % 2] = v(V.tensor_tensor(r3(prod_r, 128)[:, 0:n, :], r3(b[:, :], 128)[:, 0:n, :], OH[:, 4 * q:4 * q + n, :], ALU.mult))
                wait(V, tr[q % 2])
                last_rank[0] = v(V.tensor_reduce(rankf[:, 4 * q:4 * q + n], r3(prod_r, 128)[:, 0:n, :], AX.X, ALU.add))
            wait(V, last_rank[0])
            return v(V.tensor_copy(rank[:, 0:NT], rankf[:, 0:NT]))

        last_rank = [None]
        trow = R1[:, 10496:10496 + 196].bitcast(i32).rearrange("p (t c) -> p t c", c=4)

        t_oh = rank_1()
        t_rr = rank_2(t_oh, ps[0])
        v(V.memset(trow, 0))
        t_rk = rank_3(t_rr, [ps[4], ps[5]])
        v(V.tensor_copy(trow[:, :, 0], nodeid[:, 0:NT]))
        v(V.tensor_copy(trow[:, :, 1], rp[:, 0:NT]))
        t_tr = v(V.tensor_copy(trow[:, :, 2], deg[:, 0:NT]))
        s_tab = sem("s_tab")
        wait(G, t_tr, t_rk)
        for c in range(NT):
            t_tab = s_tab.inc(G.indirect_dma_start(out=tab_d, out_offset=bass.IndirectOffsetOnAxis(ap=rank[:, c:c + 1], axis=0),
                                                   in_=trow[:, c, :], in_offset=None), 16)
        s_tb = sem("s_tb")
        wait(Y, t_tab)
        t_tb = dma(Y, tabS, tab_d.rearrange("(t p) c -> p t c", p=128), s_tb)

        wait(V, t_w2)
        mean = R3[:, 0:32]
        wm4 = wmx.rearrange("p k (g d) -> p (k g) d", d=64)
        t = v(V.tensor_reduce(mean, wm4, AX.X, ALU.add))
        wait(V, t)
        t = v(V.tensor_scalar(out=mean, in0=mean, scalar1=1.0 / 64, scalar2=None, op0=ALU.mult))
        wait(V, t)
        t_wm = v(V.tensor_tensor(wm4, wm4, mean.unsqueeze(2).to_broadcast([128, 32, 64]), ALU.subtract))
        ksb = [R2[:, 12288 + 512 * i:12800 + 512 * i] for i in range(2)]
        vsb = [R2[:, 13312 + 512 * i:13824 + 512 * i] for i in range(2)]
        sq = R2[:, 14336:15360]
        ss, rr_ = sml[1][:, 0:16], sml[1][:, 16:32]
        t_ve, t_dt, t_ks, t_sq = {}, {}, {}, {}
        t_red = None
        dts = ps[4:8]

        def mix_dots(u):
            wait(T, t_ve[u], t_ks[u])
            for h in range(4):
                m = T.matmul(dts[h][:, 0:128], ksb[u % 2][:, h * 128:(h + 1) * 128], vsb[u % 2][:, h * 128:(h + 1) * 128],
                             start=(u == 0), stop=(u == NT - 1))
            t_dt[u] = sp.inc(m)

        for t in range(NT):
            bk_, bv_ = ps[2 * (t % 2)], ps[2 * (t % 2) + 1]
            wait(T, t_wm, t_rk, t_ve.get(t - 2), t_sq.get(t - 2), t_ks.get(t - 2))
            for b, o in ((bk_, 0), (bv_, 512)):
                for k in range(2):
                    m = T.matmul(b[:, :], xnT[:, k, t * 128:(t + 1) * 128], wmx[:, k, o:o + 512], start=(k == 0), stop=(k == 1))
            tm = sp.inc(m)
            if t > 0:
                mix_dots(t - 1)
            wait(S, tm, t_red)
            a(S.activation(sq[:, 0:512], bk_[:, :], ACT.Square))
            t_sq[t] = a(S.activation(sq[:, 512:1024], bv_[:, :], ACT.Square))
            wait(S, t_dt.get(t - 2))
            t_ks[t] = a(S.activation(ksb[t % 2], bk_[:, :], ACT.Copy))
            wait(V, t_sq[t])
            t_red = v(V.tensor_reduce(ss, r3(sq, 64), AX.X, ALU.add))
            wait(V, t_red)
            tq = v(V.tensor_scalar(out=rr_, in0=ss, scalar1=64 * EPS, scalar2=None, op0=ALU.add))
            wait(V, tq)
            tq = v(V.tensor_tensor(rr_[:, 0:8], rr_[:, 0:8], rr_[:, 8:16], ALU.mult))
            wait(S, tq)
            tq = a(S.activation(rr_[:, 0:8], rr_[:, 0:8], ACT.Sqrt))
            wait(V, tq)
            tq = v(V.reciprocal(rr_[:, 0:8], rr_[:, 0:8]))
            if t == NT - 1:
                wait(V, tq)
                tq = v(V.tensor_scalar(out=rr_[:, 0:8], in0=rr_[:, 0:8], scalar1=valid, scalar2=None, op0=ALU.mult))
            wait(V, tq, t_dt.get(t - 2))
            t_ve[t] = v(V.tensor_tensor(r3(vsb[t % 2], 64), r3(bv_[:, :], 64), rr_[:, 0:8].unsqueeze(2).to_broadcast([128, 8, 64]), ALU.mult))
        mix_dots(NT - 1)
        dsb = r3(R2[:, 6400:6912], 128)
        T1 = r3(R2[:, 6912:7936], 256)
        t = v(V.memset(dsb, 0.0))
        wait(V, t, t_dt[NT - 1])
        for h in range(4):
            for q in range(2):
                t = v(V.tensor_copy(dsb[q * 64:(q + 1) * 64, h, q * 64:(q + 1) * 64], dts[h][q * 64:(q + 1) * 64, q * 64:(q + 1) * 64]))
        wait(T, t, t_ve[NT - 1])
        for h in range(4):
            m = T.matmul(ps[h][:, 0:256], dsb[:, h, :], wq_s[:, h, :], start=True, stop=True)
        t = sp.inc(m)
        wait(V, t)
        for h in range(4):
            t = v(V.tensor_copy(T1[:, h, :], ps[h][:, 0:256]))
        wait(T, t)
        for k in range(2):
            for h in range(4):
                m = T.matmul(ps[4 + k][:, 0:256], T1[:, h, k * 128:(k + 1) * 128], wou_s[:, h, :], start=(h == 0), stop=(h == 3))
        t = sp.inc(m)
        wait(V, t)
        for k in range(2):
            t_M = v(V.tensor_scalar(out=M[:, k, :], in0=ps[4 + k][:, 0:256], scalar1=64.0 / N, scalar2=None, op0=ALU.mult))

        wait(V, t_tb)
        t = v(V.memset(degS, 0.0))
        v(V.memset(rpS, float(E)))
        wait(V, t, (sv, sv.n))
        v(V.tensor_copy(degS[:, 0:NT], tabS[:, :, 2]))
        v(V.tensor_copy(rpS[:, 0:NT], tabS[:, :, 1]))
        t_ds = v(V.tensor_copy(permS[:, 0:NT], tabS[:, :, 0]))
        wait(T, t_ds)
        t = sp.inc(T.transpose(ps[6][0:50, 0:128], degS, ident))
        wait(V, t)
        mxd = sml[2]
        t = v(V.tensor_reduce(mxd[0:50, 0:1], ps[6][0:50, 0:128], AX.X, ALU.max))
        wait(V, t)
        t = v(V.tensor_scalar(out=mxd[0:50, 1:2], in0=mxd[0:50, 0:1], scalar1=float(J - 1), scalar2=float(J), op0=ALU.add, op1=ALU.max))
        wait(V, t)
        t = v(V.tensor_copy(mxd[0:50, 2:3].bitcast(i32), mxd[0:50, 1:2]))
        wait(V, t)
        t = v(V.tensor_scalar(out=mxd[0:50, 3:4].bitcast(i32), in0=mxd[0:50, 2:3].bitcast(i32), scalar1=3, scalar2=None,
                              op0=ALU.arith_shift_right))
        wait(V, t)
        t = v(V.tensor_copy(mxd[0:50, 4:5], mxd[0:50, 3:4].bitcast(i32)))
        wait(T, t)
        t = sp.inc(T.matmul(ps[7][0:1, 0:50], mxd[0:50, 4:5], ident[0:50, 0:50], start=True, stop=True))
        wait(V, t)
        t_nch = v(V.tensor_copy(nch[0:1, 0:50], ps[7][0:1, 0:50]))

        idx0 = IDX.bitcast(i32).rearrange("p (t j) -> p t j", j=BLK)
        qs = r3(R1, 256)
        s_ix, s_q = sem("s_ix"), sem("s_q")
        srcflat = src_d
        wait(G, t_ds, t_src, t_kv[0], t_kv[1], t_kv[2])
        rpi = tabS[:, :, 1]
        t = v(V.memset(idx0[:, NT, :], 0))
        t_q49 = v(V.memset(qs[:, NT, :], 0.0))
        rpc = temp(50).bitcast(i32)
        t_rpc = v(V.tensor_copy(rpc[:, 0:NT], rpi))
        wait(G, t_rpc, t_q49)
        for c in range(NT):
            t_ix = s_ix.inc(G.indirect_dma_start(out=idx0[:, c, :], out_offset=None, in_=srcflat,
                                                 in_offset=bass.IndirectOffsetOnAxis(ap=rpc[:, c:c + 1], axis=1)), 16)
            t_qg = s_q.inc(G.indirect_dma_start(out=qs[:, c, :], out_offset=None, in_=q_d,
                                                in_offset=bass.IndirectOffsetOnAxis(ap=permS[:, c:c + 1], axis=0)), 16)

        kvb = [R2[:, i * 4096:(i + 1) * 4096].rearrange("p (j n) -> p j n", n=512) for i in range(4)]
        pv = R3[:, 0:2376].rearrange("p (j h e) -> p j h e", h=8, e=33)
        pvf = R3[:, 0:2376].rearrange("p (j n) -> p j n", n=264)
        prod = R3[:, 2400:4448]
        acc3 = acc.rearrange("p (h e) -> p h e", e=33)
        psE = ps[0]
        S3 = Sb.rearrange("p (j h) -> p j h", h=8)
        D3 = Db.rearrange("p (j h) -> p j h", h=8)
        raw = prod.rearrange("p (n d) -> p n d", d=32)

        e_arr = [sem(f"e_arr{i}").h for i in range(4)]
        e_free = [sem(f"e_free{i}").h for i in range(4)]
        e_cp, e_d, e_e, e_pv, e_pe, e_off, e_ixr, e_dm, e_end = [sem(f"e_{n}").h for n in
                                                                ("cp", "d", "e", "pv", "pe", "off", "ixr", "dm", "end")]
        e_l = [sem(f"e_l{i}").h for i in range(12)]

        loop = ExitStack()
        block = loop.enter_context(nc.Block())
        PAIRS = (NT - 1) // 2

        def blocks(e, rem, t_val, chunk, head, refetch):
            e.reg_load(rem, nch[0:1, bass.ds(t_val, 1)] if not isinstance(t_val, int) else nch[0:1, t_val:t_val + 1])
            head()
            for c in range(J):
                if c == 0:
                    chunk(c, True)
                else:
                    with e.If(e.snap(rem, min_val=-64, max_val=1 << 20) > c):
                        chunk(c, False)
            e.reg_add(rem, rem, -J)
            with e.While(lambda: e.snap(rem, min_val=-64, max_val=1 << 20) > 0):
                refetch()
                for c in range(J):
                    with e.If(e.snap(rem, min_val=-64, max_val=1 << 20) > c):
                        chunk(c, False)
                e.reg_add(rem, rem, -J)

        def regs(e, names, init):
            out_ = []
            for n, i in zip(names, init):
                r = e.alloc_register(n)
                e.reg_mov(r, i)
                out_.append(r)
            return out_

        @block.gpsimd
        def _(e):
            rem, tn, rf = regs(e, ["g_rem", "g_tn", "g_rf"], [0, 0, 0])
            use = regs(e, [f"g_u{i}" for i in range(4)], [1] * 4)
            e.wait_ge(sv.h, t_nch[1])

            def tile(t_val, par):
                def head():
                    e.reg_add(tn, tn, 1)
                    e.wait_ge(e_cp, tn)
                    e.nop().then_inc(e_dm, 1)

                def chunk(c, first):
                    b = 2 * par + c % 2
                    e.wait_ge(e_free[b], use[b])
                    e.nop().then_inc(e_dm, 1)
                    for j in range(J):
                        e.indirect_dma_start(out=kvb[b][:, j, :], out_offset=None, in_=kv_d,
                                             in_offset=bass.IndirectOffsetOnAxis(ap=ixring[par][:, c * J + j:c * J + j + 1], axis=0)
                                             ).then_inc(e_arr[b], 16)
                    e.reg_add(use[b], use[b], 1)

                def refetch():
                    e.reg_add(rf, rf, 1)
                    e.wait_ge(e_off, rf)
                    e.nop().then_inc(e_dm, 1)
                    e.indirect_dma_start(out=ixring[par], out_offset=None, in_=srcflat,
                                         in_offset=bass.IndirectOffsetOnAxis(ap=offi, axis=1)).then_inc(e_ixr, 16)
                    e.reg_mul(rfw, rf, 16)
                    e.wait_ge(e_ixr, rfw)
                    e.nop().then_inc(e_dm, 1)

                blocks(e, rem, t_val, chunk, head, refetch)

            (rfw,) = regs(e, ["g_rfw"], [16])
            tile(0, 0)
            with e.Fori(0, PAIRS) as i:
                tile(i * 2 + 1, 1)
                tile(i * 2 + 2, 0)

        @block.scalar
        def _(e):
            rem, cg = regs(e, ["a_rem", "a_g"], [0, 0])
            e.wait_ge(sv.h, sv.n)
            e.wait_ge(s_ix.h, s_ix.n)
            e.wait_ge(s_q.h, s_q.n)

            def copies(t_val, par):
                sl = (lambda n: bass.ds(t_val, n)) if not isinstance(t_val, int) else (lambda n: slice(t_val, t_val + n))
                e.activation(qring[par], qs[:, sl(1), :].rearrange("p a d -> p (a d)"), ACT.Copy)
                e.activation(ixring[par], idx0[:, sl(1), :].rearrange("p a d -> p (a d)"), ACT.Copy)
                e.activation(degring[par], degS[:, sl(1)], ACT.Copy)
                e.activation(rpring[par], rpS[:, sl(1)], ACT.Copy).then_inc(e_cp, 1)

            def tile(t_val, par):
                def chunk(c, first):
                    e.reg_add(cg, cg, 1)
                    e.wait_ge(e_d, cg)
                    e.activation(pv[:, :, :, 32], D3, ACT.Exp).then_inc(e_e, 1)
                    if first:
                        copies(t_val + 1, 1 - par)

                blocks(e, rem, t_val, chunk, lambda: None, lambda: None)

            copies(0, 0)
            tile(0, 0)
            with e.Fori(0, PAIRS) as i:
                tile(i * 2 + 1, 1)
                tile(i * 2 + 2, 0)

        @block.tensor
        def _(e):
            rem, cg = regs(e, ["t_rem", "t_g"], [0, 0])
            e.wait_ge(sv.h, t_nch[1])

            def tile(t_val):
                def chunk(c, first):
                    e.reg_add(cg, cg, 1)
                    e.wait_ge(e_pv, cg)
                    for j in range(J):
                        m = e.matmul(psE[:, 0:264], ident, pvf[:, j, :], start=(j == 0), stop=(j == J - 1))
                    m.then_inc(e_pe, 1)

                blocks(e, rem, t_val, chunk, lambda: None, lambda: None)

            tile(0)
            with e.Fori(0, PAIRS) as i:
                tile(i * 2 + 1)
                tile(i * 2 + 2)

        @block.vector
        def _(e):
            rem, cg, gm, tn, of = regs(e, ["v_rem", "v_g", "v_gm", "v_tn", "v_of"], [0, 0, 0, 0, 0])
            arr = regs(e, [f"v_a{i}" for i in range(4)], [0] * 4)
            e.wait_ge(sv.h, sv.n)
            e.wait_ge(s_ix.h, s_ix.n)
            e.wait_ge(s_q.h, s_q.n)
            for b in range(4):
                e.nop().then_inc(e_free[b], 1)
            e.memset(acc, 0.0)
            e.memset(pv[:, :, :, 32], 0.0)
            e.memset(S3[:, J, :], -0.1 * BIG).then_inc(e_l[0], 1)
            e.wait_ge(e_l[0], 1)

            def flush(reg):
                e.wait_ge(e_pe, gm)
                e.tensor_tensor(acc3, acc3, pv[:, J, :, 32].unsqueeze(2).to_broadcast([128, 8, 33]), ALU.mult).then_inc(e_l[1], 1)
                e.wait_ge(e_l[1], gm)
                e.tensor_tensor(acc, acc, psE[:, 0:264], ALU.add).then_inc(e_l[2], 1)
                e.wait_ge(e_l[2], gm)

            def finish(t_val):
                e.tensor_scalar(out=rin, in0=acc3[:, :, 32], scalar1=1e-30, scalar2=None, op0=ALU.max).then_inc(e_l[3], 1)
                e.wait_ge(e_l[3], tn)
                e.reciprocal(rin, rin).then_inc(e_l[4], 1)
                e.wait_ge(e_l[4], tn)
                dst_ = (qs[:, bass.ds(t_val, 1), :] if not isinstance(t_val, int) else qs[:, t_val:t_val + 1, :])
                e.tensor_tensor(dst_.rearrange("p a (h d) -> p (a h) d", d=32), acc3[:, :, 0:32],
                                rin.unsqueeze(2).to_broadcast([128, 8, 32]), ALU.mult).then_inc(e_l[5], 1)
                e.wait_ge(e_l[5], tn)

            def mask(par):
                return e.tensor_scalar(out=maskb, in0=iota[:, 0:BLK], scalar1=degring[par], scalar2=-BIG, op0=ALU.is_ge, op1=ALU.mult)

            def tile(t_val, par, start):
                def head():
                    if not start:
                        e.reg_add(tn, tn, 1)
                    e.reg_add(tp, tp, 1)
                    e.wait_ge(e_cp, tp)
                    mask(par).then_inc(e_l[6], 1)

                def chunk(c, first):
                    b = 2 * par + c % 2
                    e.reg_mov(gm, cg)
                    e.reg_add(cg, cg, 1)
                    e.reg_add(arr[b], arr[b], 16 * J)
                    e.wait_ge(e_arr[b], arr[b])
                    e.tensor_tensor(prod.rearrange("p (j n) -> p j n", n=256), kvb[b][:, :, 0:256],
                                    qring[par].unsqueeze(1).to_broadcast([128, J, 256]), ALU.mult).then_inc(e_l[7], 1)
                    e.wait_ge(e_l[7], cg)
                    e.tensor_reduce(Sb[:, 0:64], raw, AX.X, ALU.add).then_inc(e_l[8], 1)
                    if not (start and first):
                        flush(gm)
                    e.wait_ge(e_l[0], cg)
                    if first and not start:
                        finish(t_val - 1)
                        e.memset(S3[:, J, :], -0.1 * BIG)
                        e.memset(acc, 0.0).then_inc(e_l[11], 1)
                        e.wait_ge(e_l[11], tn)
                    if first:
                        e.wait_ge(e_l[6], mk)
                    e.wait_ge(e_l[8], cg)
                    e.tensor_tensor(S3[:, 0:J, :], S3[:, 0:J, :], maskb[:, c * J:(c + 1) * J].unsqueeze(2).to_broadcast([128, J, 8]),
                                    ALU.add).then_inc(e_l[9], 1)
                    e.wait_ge(e_l[9], cg)
                    e.tensor_reduce(mnew, Sb.rearrange("p (j h) -> p h j", h=8), AX.X, ALU.max).then_inc(e_l[10], 1)
                    e.wait_ge(e_l[10], cg)
                    e.tensor_tensor(D3, S3, mnew.unsqueeze(1).to_broadcast([128, J + 1, 8]), ALU.subtract).then_inc(e_d, 1)
                    e.wait_ge(e_d, cg)
                    e.tensor_copy(S3[:, J, :], mnew).then_inc(e_l[0], 1)
                    e.wait_ge(e_e, cg)
                    e.tensor_tensor(pv[:, 0:J, :, 0:32], kvb[b][:, :, 256:512].rearrange("p j (h d) -> p j h d", d=32),
                                    pv[:, 0:J, :, 32].unsqueeze(3).to_broadcast([128, J, 8, 32]), ALU.mult).then_inc(e_pv, 1)
                    e.wait_ge(e_pv, cg)
                    e.nop().then_inc(e_free[b], 1)

                def refetch():
                    e.reg_add(of, of, 1)
                    e.tensor_scalar(out=degring[par], in0=degring[par], scalar1=-float(BLK), scalar2=None, op0=ALU.add)
                    e.tensor_scalar(out=rpring[par], in0=rpring[par], scalar1=float(BLK), scalar2=float(E), op0=ALU.add,
                                    op1=ALU.min).then_inc(e_end, 1)
                    e.wait_ge(e_end, of)
                    mask(par).then_inc(e_l[6], 1)
                    e.reg_add(mk, mk, 1)
                    e.wait_ge(e_l[6], mk)
                    e.tensor_copy(offi, rpring[par]).then_inc(e_off, 1)

                e.reg_add(mk, mk, 1)
                blocks(e, rem, t_val, chunk, head, refetch)

            tp, mk = regs(e, ["v_tp", "v_mk"], [0, 0])
            tile(0, 0, True)
            with e.Fori(0, PAIRS) as i:
                tile(i * 2 + 1, 1, False)
                tile(i * 2 + 2, 0, False)
            e.reg_mov(gm, cg)
            e.reg_add(tn, tn, 1)
            flush(gm)
            finish(NT - 1)
            e.nop().then_inc(sv.h, 1)
            sv.n += 1


        loop.close()
        t_fin = (sv, sv.n)

        s_ag = sem("s_ag")
        wait(G, t_fin)
        for c in range(NT):
            t_ag = s_ag.inc(G.indirect_dma_start(out=agg_d, out_offset=bass.IndirectOffsetOnAxis(ap=permS[:, c:c + 1], axis=0),
                                                 in_=qs[:, c, :], in_offset=None), 16)
        abuf = [r3(R2[:, 12544 + 1792 * i:12544 + 1792 * (i + 1)], 256) for i in range(2)]
        xres = [r3(R3[:, 1792 * i:1792 * (i + 1)], 256) for i in range(2)]
        s_ab = [sem("s_ab0"), sem("s_ab1")]
        x2 = r3(R1[:, 0:12544], 256)
        hh = r3(R2[:, 0:12544], 256)
        aT = [r3(IDX[:, 256 * i:256 * (i + 1)], 128) for i in range(2)]
        hT = [r3(IDX[:, 512 + 256 * i:768 + 256 * i], 128) for i in range(2)]
        L, Ex, oh, q1, q2 = [IDX[:, 1024 + 392 * i:1416 + 392 * i] for i in range(5)]
        wait(V, t_fin)
        t_mx = None

        obias, obias2 = R3[0:1, 3584:3840], R3[0:1, 3840:4096]
        s_ob = sem("s_ob")
        wait(Y, t_fin)
        dma(Y, obias, row(bo), s_ob)
        t_ob = dma(Y, obias2, row(b_out), s_ob)

        def load_e(grp):
            b = grp % 2
            wait(Y, t_ag, t_mx)
            dma(Y, abuf[b], agg_d[grp * 896:(grp + 1) * 896, :].rearrange("(t p) d -> p t d", p=128), s_ab[b])
            if grp < 6:
                return dma(Y, xres[b], x[grp * 896:(grp + 1) * 896, :].rearrange("(t p) d -> p t d", p=128), s_ab[b])
            dma(Y, xres[b][:, 0:6, :], x[grp * 896:grp * 896 + 768, :].rearrange("(t p) d -> p t d", p=128), s_ab[b])
            return dma(Y, xres[b][0:N - 48 * 128, 6, :], x[48 * 128:N, :], s_ab[b])

        t_e = {0: load_e(0), 1: load_e(1)}
        t_aT, t_ps, t_x2, t_hT, t_lg, t_ld, t_hp = {}, {}, {}, {}, {}, {}, {}

        def gate(u):
            pt = ps[4 + u % 2]
            wait(T, t_h[u // 7], t_hT.get(u - 2))
            for k in range(2):
                m = T.transpose(pt[:, k * 128:(k + 1) * 128], hh[:, u, k * 128:(k + 1) * 128], ident)
            t_ = sp.inc(m)
            wait(S, t_, t_lg.get(u - 2))
            t_hT[u] = a(S.activation(hT[u % 2], r3(pt[:, 0:256], 128), ACT.Copy))
            wait(T, t_hT[u], t_ld.get(u - 2))
            for k in range(2):
                m = T.matmul(ps[6 + u % 2][:, 0:8], hT[u % 2][:, k, :], gw[:, k, :], start=(k == 0), stop=(k == 1))
            t_lg[u] = sp.inc(m)
            wait(V, t_lg[u])
            t_ld[u] = v(V.tensor_tensor(L[:, u * 8:(u + 1) * 8], ps[6 + u % 2][:, 0:8], gbias, ALU.add))

        t_h = {}
        for grp in range(7):
            for j in range(7):
                t = grp * 7 + j
                pt = ps[t % 2]
                wait(T, t_e[grp], t_aT.get(t - 2))
                for k in range(2):
                    m = T.transpose(pt[:, k * 128:(k + 1) * 128], abuf[grp % 2][:, j, k * 128:(k + 1) * 128], ident)
                t_tp[t] = sp.inc(m)
                wait(S, t_tp[t], t_ps.get(t - 2))
                t_aT[t] = a(S.activation(aT[t % 2], r3(pt[:, 0:256], 128), ACT.Copy))
                wait(T, t_x2.get(t - 2), t_M)
                po = ps[2 + t % 2][:, 0:256]
                wait(T, t_ob)
                T.matmul(po, ones[0:1, :], obias, start=True, stop=False)
                T.matmul(po, ones[0:1, :], obias2, start=False, stop=False)
                for k in range(2):
                    T.matmul(po, xnT[:, k, t * 128:(t + 1) * 128], M[:, k, :], start=False, stop=False)
                wait(T, t_aT[t])
                for k in range(2):
                    m = T.matmul(po, aT[t % 2][:, k, :], wo_s[:, k, :], start=False, stop=(k == 1))
                t_ps[t] = sp.inc(m)
                wait(V, t_ps[t], t_e[grp])
                t_x2[t] = v(V.tensor_tensor(x2[:, t, :], po, xres[grp % 2][:, j, :], ALU.add))
            wait(V, t_x2[grp * 7 + 6])
            t_h[grp] = norm(x2[:, grp * 7:grp * 7 + 7, :], 7, hh[:, grp * 7:grp * 7 + 7, :])
            if grp + 2 < 7:
                wait(Y, t_x2[grp * 7 + 6], t_tp[grp * 7 + 6])
                if grp + 2 == 6:
                    t_mx = v(V.memset(xres[0][:, 6, :], 0.0))
                t_e[grp + 2] = load_e(grp + 2)
            if grp > 0:
                for u in range(grp * 7 - 7, grp * 7):
                    gate(u)
        for u in range(42, 49):
            gate(u)

        e3 = lambda ap: r3(ap, 8)
        bc = lambda col: col.unsqueeze(2).to_broadcast([128, NT, 8])
        rowe = lambda r: r.unsqueeze(1).to_broadcast([128, NT, 8])
        mx, sm, pm, wv, pos, kept, bs, rev, off8 = [R3[:, 4096 + o_:4096 + o_ + w_] for o_, w_ in ((0, 49), (49, 49), (98, 49), (147, 49), (196, 49), (245, 49), (294, 49), (343, 8), (351, 8))]
        v(V.tensor_scalar(out=rev, in0=iota[:, 0:8], scalar1=-1.0, scalar2=8.0, op0=ALU.mult, op1=ALU.add))
        v(V.tensor_scalar(out=off8, in0=iota[:, 0:8], scalar1=float(CP), scalar2=None, op0=ALU.mult))

        def seq(ins):
            wait(V, v(ins))

        wait(V, t_ld[48])
        seq(V.tensor_reduce(mx, e3(L), AX.X, ALU.max))
        t = v(V.tensor_tensor(e3(L), e3(L), bc(mx), ALU.subtract))
        wait(S, t)
        t = a(S.activation(Ex, L, ACT.Exp))
        wait(V, t)
        seq(V.tensor_reduce(sm, e3(Ex), AX.X, ALU.add))
        seq(V.reciprocal(sm, sm))
        seq(V.tensor_tensor(e3(Ex), e3(Ex), bc(sm), ALU.mult))
        seq(V.tensor_reduce(pm, e3(Ex), AX.X, ALU.max))
        seq(V.tensor_tensor(e3(q1), e3(Ex), bc(pm), ALU.is_equal))
        seq(V.tensor_tensor(e3(q1), e3(q1), rowe(rev), ALU.mult))
        seq(V.tensor_reduce(wv, e3(q1), AX.X, ALU.max))
        seq(V.tensor_tensor(e3(oh), bc(wv), rowe(rev), ALU.is_equal))
        seq(V.tensor_scalar(out=e3(oh)[:, 48, :], in0=e3(oh)[:, 48, :], scalar1=valid, scalar2=None, op0=ALU.mult))
        seq(V.memset(e3(q2)[:, 0, :], 0.0))
        for c in range(NT - 1):
            seq(V.tensor_tensor(e3(q2)[:, c + 1, :], e3(q2)[:, c, :], e3(oh)[:, c, :], ALU.add))
        wait(T, (sv, sv.n))
        T.matmul(ps[0][:, 0:392], ones, q2, start=True, stop=False)
        t = sp.inc(T.matmul(ps[0][:, 0:392], tri, oh, start=False, stop=True))
        wait(V, t)
        seq(V.tensor_tensor(q1, ps[0][:, 0:392], oh, ALU.mult))
        seq(V.tensor_reduce(pos, e3(q1), AX.X, ALU.add))
        seq(V.tensor_tensor(e3(q1), e3(oh), rowe(off8), ALU.mult))
        seq(V.tensor_reduce(bs, e3(q1), AX.X, ALU.add))
        seq(V.tensor_scalar(out=kept, in0=pos, scalar1=float(C), scalar2=None, op0=ALU.is_lt))
        seq(V.tensor_scalar(out=kept[:, 48:49], in0=kept[:, 48:49], scalar1=valid, scalar2=None, op0=ALU.mult))
        v(V.tensor_tensor(coef[:, 0:NT], pm, kept, ALU.mult))
        seq(V.tensor_scalar(out=mx, in0=kept, scalar1=-16384.0, scalar2=16384.0, op0=ALU.mult, op1=ALU.add))
        seq(V.tensor_tensor(mx, mx, pos, ALU.add))
        seq(V.tensor_tensor(mx, mx, bs, ALU.add))
        t_sl = v(V.tensor_copy(slotS[:, 0:NT], mx))
        seq(V.tensor_scalar(out=pos, in0=pos, scalar1=float(C - 1), scalar2=None, op0=ALU.min))
        seq(V.scalar_tensor_tensor(out=pos, in0=bs, scalar=C / CP, in1=pos, op0=ALU.mult, op1=ALU.add))
        t_sg = v(V.tensor_copy(slotG[:, 0:NT], pos))
        s_sc = sem("s_sc")
        wait(G, t_sl, t_hz, t_h[6])
        for c in range(NT):
            t_sc = s_sc.inc(G.indirect_dma_start(out=hb_d, out_offset=bass.IndirectOffsetOnAxis(ap=slotS[:, c:c + 1], axis=0),
                                                 in_=hh[:, c, :], in_offset=None, bounds_check=H * CP - 1, oob_is_err=False), 16)

        w1b = [r3(R0[:, 2048 * i:2048 * (i + 1)], 1024) for i in range(2)]
        w2b = [r3(R0[:, 4096 + 2048 * i:4096 + 2048 * (i + 1)], 256) for i in range(2)]
        b1_s = R0[:, 8192:8256]
        b2_s = R0[0:1, 8256:8256 + 2048]
        hmid = r3(R2[:, 0:8192], 1024)
        rowb = [r3(R2[:, 8192 + 2048 * i:8192 + 2048 * (i + 1)], 256) for i in range(2)]
        xT = [r3(R2[:, 12288 + 2048 * i:12288 + 2048 * (i + 1)], 1024) for i in range(2)]
        yst = [r3(R3[:, 2048 * i:2048 * (i + 1)], 256) for i in range(2)]
        s_we = [sem("s_we0"), sem("s_we1")]
        s_re = [sem("s_re0"), sem("s_re1")]
        s_ye = [sem("s_ye0"), sem("s_ye1")]
        s_b = sem("s_b")
        wait(Y, t_ps[48], t_x2[48])
        dma(Y, b1_s, b1, s_b)
        t_bb = dma(Y, b2_s, b2.rearrange("(a e) d -> a (e d)", a=1), s_b)
        t_l1, t_l2, t_xp, t_xc, t_y = {}, {}, {}, {}, {}

        def load_w(e):
            b = e % 2
            wait(Y, t_l1.get(e - 2), t_l2.get(e - 2))
            dma(Y, w1b[b], kpart(w1[e]), s_we[b])
            return dma(Y, w2b[b], kpart(w2[e]), s_we[b])

        def load_r(e):
            wait(Y, t_sc, t_xp.get(e - 2))
            return dma(Y, rowb[e % 2], hb_d[e * CP:(e + 1) * CP, :].rearrange("(j p) d -> p j d", p=128), s_re[e % 2])

        t_wl = {0: load_w(0), 1: load_w(1)}
        t_rl = {0: load_r(0), 1: load_r(1)}
        bank_free = {}

        def turn(e):
            wait(T, t_rl[e])
            for k in range(2):
                for jj in range(2):
                    i = k * 2 + jj
                    b = ps[i % 2]
                    wait(T, bank_free.get(i % 2))
                    for j in range(4):
                        m = T.transpose(b[:, j * 128:(j + 1) * 128], rowb[e % 2][:, jj * 4 + j, k * 128:(k + 1) * 128], ident)
                    t_xp[e] = sp.inc(m)
                    wait(V, t_xp[e], t_l1.get(e - 2))
                    bank_free[i % 2] = v(V.tensor_copy(xT[e % 2][:, k, jj * 512:(jj + 1) * 512], b[:, :]))
            t_xc[e] = bank_free[1]

        COLS = [(0, 489), (489, 488)]
        turn(0)
        t_l = None
        wait(S, t_bb)
        for e in range(8):
            if e > 0 and e + 1 < 8:
                t_wl[e + 1] = load_w(e + 1)
                t_rl[e + 1] = load_r(e + 1)
            wait(T, t_xc[e], t_wl[e], t_bb)
            for f in range(8):
                for n, (c0, cw) in enumerate(COLS):
                    i = 2 + (f * 2 + n) % 4
                    wait(T, bank_free.get(i))
                    for k in range(2):
                        m = T.matmul(ps[i][:, 0:cw], w1b[e % 2][:, k, f * 128:(f + 1) * 128], xT[e % 2][:, k, c0:c0 + cw],
                                     start=(k == 0), stop=(k == 1))
                    t = sp.inc(m)
                    wait(S, t, t_l2.get(e - 1))
                    bank_free[i] = t_l = a(S.activation(hmid[:, f, c0:c0 + cw], ps[i][:, 0:cw], ACT.Relu,
                                                        bias=b1_s[:, e * 8 + f:e * 8 + f + 1]))
            t_l1[e] = t
            if e + 1 < 8:
                turn(e + 1)
            wait(T, t_l)
            for j in range(8):
                i = 6 + j % 2
                m_ = 128 if j < 7 else C - 896
                wait(T, bank_free.get(i))
                T.matmul(ps[i][0:m_, 0:256], ones[0:1, 0:m_], b2_s[:, e * 256:(e + 1) * 256], start=True, stop=False)
                for f in range(8):
                    m = T.matmul(ps[i][0:m_, 0:256], hmid[:, f, j * 128:j * 128 + m_], w2b[e % 2][:, f, :], start=False, stop=(f == 7))
                t_l2[e] = sp.inc(m)
                wait(V, t_l2[e], t_y.get(e - 2))
                bank_free[i] = v(V.tensor_copy(yst[e % 2][0:m_, j, :], ps[i][0:m_, 0:256]))
            wait(Y, bank_free[7])
            dma(Y, yb_d[e * C:e * C + 896, :].rearrange("(j p) d -> p j d", p=128), yst[e % 2][:, 0:7, :], s_ye[e % 2])
            t_y[e] = dma(Y, yb_d[e * C + 896:(e + 1) * C, :], yst[e % 2][0:C - 896, 7, :], s_ye[e % 2])

        gb = r3(R2[:, 0:12544], 256)
        s_gb = [sem(f"s_gb{i}") for i in range(7)]
        s_out = sem("s_out")
        wait(G, t_sg, t_y[6], t_y[7], t_l2[7], t_xp[7])
        for c in range(NT):
            t_gb = s_gb[c // 7].inc(G.indirect_dma_start(out=gb[:, c, :], out_offset=None, in_=yb_d,
                                                        in_offset=bass.IndirectOffsetOnAxis(ap=slotG[:, c:c + 1], axis=0)), 16)
        n_ = 7 * 256
        u1 = R3[:, 0:n_]
        u2 = R3[:, n_:2 * n_]
        wait(V, t_y[6], t_y[7])
        for grp in range(7):
            wait(V, (s_gb[grp], 16 * 7))
            y = R2[:, grp * n_:(grp + 1) * n_]
            for j in range(7):
                c = grp * 7 + j
                t = v(V.tensor_scalar(out=gb[:, c, :], in0=gb[:, c, :], scalar1=coef[:, c:c + 1], scalar2=None, op0=ALU.mult))
            wait(V, t)
            v(V.tensor_scalar(out=u1, in0=y, scalar1=0.0, scalar2=1e4, op0=ALU.is_gt, op1=ALU.mult))
            t = v(V.tensor_scalar(out=u2, in0=y, scalar1=0.0, scalar2=-1e4, op0=ALU.is_lt, op1=ALU.mult))
            wait(V, t)
            seq(V.tensor_tensor(u1, u1, u2, ALU.add))
            seq(V.tensor_scalar(out=u2, in0=y, scalar1=0.0, scalar2=0.0, op0=ALU.mult, op1=ALU.not_equal))
            seq(V.copy_predicated(y, u2.bitcast(i32), u1))
            t = v(V.tensor_tensor(y, y, R1[:, grp * n_:(grp + 1) * n_], ALU.add))
            wait(Y, t)
            if grp < 6:
                dma(Y, out[grp * 896:(grp + 1) * 896, :].rearrange("(t p) d -> p t d", p=128), gb[:, grp * 7:grp * 7 + 7, :], s_out)
            else:
                dma(Y, out[grp * 896:grp * 896 + 768, :].rearrange("(t p) d -> p t d", p=128), gb[:, 42:48, :], s_out)
                t_out = dma(Y, out[48 * 128:N, :], gb[0:N - 48 * 128, 48, :], s_out)
        wait(Y, t_out, *[(s_, s_.n) for s_ in s_ye], (s_ed, s_ed.n), (s_pz, s_pz.n), (s_hz, s_hz.n), (s_tab, s_tab.n),
             (s_ag, s_ag.n), (s_sc, s_sc.n), *[(s_, s_.n) for s_ in s_st])


def kernel(x, src, dst, edge_weight1, L0_gnn_Wq, L0_gnn_bq, L0_gnn_Wk, L0_gnn_bk, L0_gnn_Wv, L0_gnn_bv, L0_gnn_Wo,
           L0_gnn_bo, L0_mix_w_qkv, L0_mix_w_out, L0_mix_b_out, L0_ffn_gate_w, L0_ffn_gate_b, L0_ffn_w1, L0_ffn_b1,
           L0_ffn_w2, L0_ffn_b2):
    import numpy as np
    import concourse.bacc as bacc
    from concourse.bass_utils import run_bass_kernel_spmd

    n = np.asarray
    wqkv = n(L0_mix_w_qkv)
    arrays = {
        "x": n(x), "src": n(src), "dst": n(dst),
        "wall": np.concatenate([n(L0_gnn_Wk).T, n(L0_gnn_Wv).T, n(L0_gnn_Wq).T], axis=1),
        "ball": np.concatenate([n(L0_gnn_bk), n(L0_gnn_bv), n(L0_gnn_bq)]),
        "wmix": wqkv[512:].T, "wqm": wqkv[:512], "wout": n(L0_mix_w_out).T, "wo": n(L0_gnn_Wo).T,
        "bo": n(L0_gnn_bo), "b_out": n(L0_mix_b_out), "gate_w": n(L0_ffn_gate_w), "gate_b": n(L0_ffn_gate_b),
        "w1": n(L0_ffn_w1), "b1": n(L0_ffn_b1).reshape(8, 8, 128).transpose(2, 0, 1).reshape(128, 64),
        "w2": n(L0_ffn_w2), "b2": n(L0_ffn_b2),
    }
    nc = bacc.Bacc("TRN2", target_bir_lowering=False, num_devices=1)
    args, feed = [], {}
    for name, arr in arrays.items():
        arr = np.ascontiguousarray(arr)
        feed["in_" + name] = arr
        args.append(nc.dram_tensor("in_" + name, arr.shape, mybir.dt.from_np(arr.dtype), kind="ExternalInput").ap())
    out = nc.dram_tensor("out_0", (N, D), mybir.dt.float32, kind="ExternalOutput").ap()
    gps_layer_kernel(nc, *args, out)
    r = run_bass_kernel_spmd(nc, [feed], core_ids=[0])
    return r.results[0]["out_0"]
```
